# Optimizing a Trainium2 kernel written in Bass

```python
import numpy as np
import jax
import jax.numpy as jnp

def _softmax(x, axis=-1):
    return jax.nn.softmax(x, axis=axis)

def _gelu(x):
    return jax.nn.gelu(x, approximate=True)

def _silu(x):
    return jax.nn.silu(x)

def _sigmoid(x):
    return jax.nn.sigmoid(x)

def _layernorm(x, axis=-1, eps=1e-05):
    m = jnp.mean(x, axis=axis, keepdims=True)
    v = jnp.var(x, axis=axis, keepdims=True)
    return (x - m) / jnp.sqrt(v + eps)

def _scatter_add(tgt, idx, src, axis=0):
    return tgt.at[idx].add(src)

def _segment_sum(src, seg, n):
    return jax.ops.segment_sum(src, seg, n)
kernel_name = 'mk_cond_seq_d1_seqx_r2_b93546'

def setup_inputs(seed: int=0):
    np.random.seed(seed)
    _w = jnp.asarray

    def _rec_inputs():
        import jax
        import jax.numpy as jnp
        _rk = jax.random.key(seed)
        x = -1.528e-05 + 0.9999 * jax.random.normal(jax.random.fold_in(_rk, 1), (8, 512, 1024), jnp.float32)
        _lenS = 512 - jax.random.randint(jax.random.fold_in(_rk, 7), (8,), 0, max(1, 512 // 4) + 1, jnp.int32)
        _lenS2 = 512 - jax.random.randint(jax.random.fold_in(_rk, 8), (8,), 0, max(1, 512 // 4) + 1, jnp.int32)
        itok_B_1_2 = jax.random.randint(jax.random.fold_in(_rk, 11), (8,), 1, 3, jnp.int32)
        return (x, itok_B_1_2)
    x, itok_B_1_2 = _rec_inputs()

    def _L0_cond_setup():
        import jax, jax.numpy as jnp
        import numpy as np
        H = 1024
        K = 512
        R = 3
        B = 8
        S = 1024
        LN_EPS = 1e-05
        key = jax.random.key(seed)
        ks = jax.random.split(key, 8)
        sd_d = 1.0 / np.sqrt(H)
        sd_u = 1.0 / np.sqrt(K)
        return {'role': jax.random.randint(ks[0], (B,), 0, R), 'hidden_states': jax.random.normal(ks[1], (B, S, H), dtype=jnp.float32), 'W_down': jax.random.uniform(ks[2], (R, H, K), jnp.float32, -sd_d, sd_d), 'b_down': jax.random.uniform(ks[3], (R, K), jnp.float32, -sd_d, sd_d), 'W_up': jax.random.uniform(ks[4], (R, K, H), jnp.float32, -sd_u, sd_u), 'b_up': jax.random.uniform(ks[5], (R, H), jnp.float32, -sd_u, sd_u), 'gamma': jnp.ones((R, H), jnp.float32), 'beta': jnp.zeros((R, H), jnp.float32)}
    _L0_cond_all = _L0_cond_setup()
    _L0_cond_in = {k: v for k, v in _L0_cond_all.items() if k in ('W_down', 'b_down', 'W_up', 'b_up', 'gamma', 'beta')}
    del _L0_cond_all
    return {'x': x, 'itok_B_1_2': itok_B_1_2, 'L0_cond_W_down': _L0_cond_in['W_down'], 'L0_cond_b_down': _L0_cond_in['b_down'], 'L0_cond_W_up': _L0_cond_in['W_up'], 'L0_cond_b_up': _L0_cond_in['b_up'], 'L0_cond_gamma': _L0_cond_in['gamma'], 'L0_cond_beta': _L0_cond_in['beta']}

def reference(x, itok_B_1_2, L0_cond_W_down, L0_cond_b_down, L0_cond_W_up, L0_cond_b_up, L0_cond_gamma, L0_cond_beta):
    import jax
    import jax.numpy as jnp

    def _L0_cond_ref(role, hidden_states, W_down, b_down, W_up, b_up, gamma, beta):
        import jax, jax.numpy as jnp
        import numpy as np
        H = 1024
        K = 512
        R = 3
        B = 8
        S = 1024
        LN_EPS = 1e-05
        h = jnp.einsum('bsh,bhk->bsk', hidden_states, W_down[role]) + b_down[role][:, None, :]
        h = jax.nn.gelu(h, approximate=False)
        u = jnp.einsum('bsk,bkh->bsh', h, W_up[role]) + b_up[role][:, None, :]
        y = hidden_states + u
        mean = jnp.mean(y, axis=-1, keepdims=True)
        var = jnp.mean(jnp.square(y - mean), axis=-1, keepdims=True)
        yn = (y - mean) * jax.lax.rsqrt(var + LN_EPS)
        return yn * gamma[role][:, None, :] + beta[role][:, None, :]
    x = _L0_cond_ref(itok_B_1_2, x, L0_cond_W_down, L0_cond_b_down, L0_cond_W_up, L0_cond_b_up, L0_cond_gamma, L0_cond_beta)
    return x

_drawn_inputs = setup_inputs


def setup_inputs(seed=0):
    import zlib

    import numpy as np

    out = dict(_drawn_inputs(seed))
    spreads = {'L0_cond_gamma': (1.0, 0.2), 'L0_cond_beta': (0.0, 0.1)}
    factors = {'L0_cond_b_down': 8.0}
    for name, (base, spread) in spreads.items():
        noise = np.random.default_rng([zlib.crc32(name.encode()), seed]).standard_normal(out[name].shape)
        drawn = base * np.exp(spread * noise) if base else spread * noise
        out[name] = jnp.asarray(drawn.astype(out[name].dtype))
    for name, factor in factors.items():
        out[name] = (out[name] * factor).astype(out[name].dtype)
    return out
```

```python
from contextlib import ExitStack

import concourse.bass as bass
from concourse import mybir

P = 128
LN_EPS = 1e-05

ALU = mybir.AluOpType
ACT = mybir.ActivationFunctionType
F32 = mybir.dt.float32
F32R = mybir.dt.float32r
I32 = mybir.dt.int32


def bass_role_adapter_layernorm(
    nc: bass.Bass,
    x: bass.AP,
    xT: bass.AP,
    roles: bass.AP,
    W_down: bass.AP,
    b_down_cols: bass.AP,
    W_up: bass.AP,
    b_up: bass.AP,
    gamma: bass.AP,
    beta: bass.AP,
    out: bass.AP,
):
    B, S, H = x.shape
    R, _, K = W_down.shape
    HC = H // P
    KC = K // P
    NT = S // P
    NLOAD = 4
    CPL = HC // NLOAD
    BANK = 512
    HALVES = H // BANK
    NSTAGE = 2
    assert KC == NLOAD and S == BANK and K == BANK and HALVES == 2 and NT == 4

    with ExitStack() as ctx:
        def sb(name, shape, dt):
            return ctx.enter_context(nc.sbuf_tensor(name, shape, dt))

        def sem(name):
            return ctx.enter_context(nc.semaphore(name))

        x_stage = sb("x_stage", [P, NSTAGE, CPL * S], F32)
        wd_stage = sb("wd_stage", [P, NSTAGE, CPL * K], F32)
        wu_stage = sb("wu_stage", [P, NSTAGE, H], F32)
        x_hi = sb("x_hi", [P, NLOAD, CPL * S], F32R)
        x_lo = sb("x_lo", [P, NLOAD, CPL * S], F32R)
        wd_hi = sb("wd_hi", [P, NLOAD, CPL * K], F32R)
        wd_lo = sb("wd_lo", [P, NLOAD, CPL * K], F32R)
        wu_hi = sb("wu_hi", [P, KC, H], F32R)
        wu_lo = sb("wu_lo", [P, KC, H], F32R)
        h_full = sb("h_full", [P, KC, S], F32)
        h_hi = sb("h_hi", [P, KC, S], F32R)
        h_lo = sb("h_lo", [P, KC, S], F32R)
        rows = sb("rows", [P, NT, H], F32)
        b_up_all = sb("b_up_all", [P, R * H], F32)
        gamma_all = sb("gamma_all", [P, R * H], F32)
        beta_all = sb("beta_all", [P, R * H], F32)
        b_down_all = sb("b_down_all", [P, R * KC], F32)
        roles_sb = sb("roles_sb", [1, B], I32)
        bn_parts = sb("bn_parts", [P, NT, HALVES, 6], F32)
        mean_var = sb("mean_var", [P, NT, 2], F32)
        var_eps = sb("var_eps", [P, NT], F32)
        rstd = sb("rstd", [P, NT], F32)
        eps = sb("eps", [P, 1], F32)
        minus_half = sb("minus_half", [P, 1], F32)

        down_ps = ctx.enter_context(nc.psum_tensor("down_ps", [P, KC, BANK], F32))
        up_ps = ctx.enter_context(nc.psum_tensor("up_ps", [P, 2, H], F32))

        roles_landed = sem("roles_landed")
        b_down_landed = sem("b_down_landed")
        b_up_landed = sem("b_up_landed")
        gamma_landed = sem("gamma_landed")
        beta_landed = sem("beta_landed")
        x_landed = [sem(f"x_landed{i}") for i in range(NSTAGE)]
        wd_landed = [sem(f"wd_landed{i}") for i in range(NSTAGE)]
        wu_landed = [sem(f"wu_landed{i}") for i in range(NSTAGE)]
        rows_landed = [sem(f"rows_landed{t}") for t in range(NT)]
        stored = [sem(f"stored{t}") for t in range(NT)]
        x_hi_ready = sem("x_hi_ready")
        wd_hi_ready = sem("wd_hi_ready")
        wu_hi_ready = sem("wu_hi_ready")
        h_full_ready = sem("h_full_ready")
        h_hi_ready = sem("h_hi_ready")
        x_split = sem("x_split")
        wd_split = sem("wd_split")
        wu_split = sem("wu_split")
        h_split = sem("h_split")
        d_part_used = sem("d_part_used")
        down_ready = sem("down_ready")
        up_ready = sem("up_ready")
        biased = sem("biased")
        summed = sem("summed")
        bn_ready = sem("bn_ready")
        mean_ready = sem("mean_ready")
        constants_ready = sem("constants_ready")
        var_eps_ready = sem("var_eps_ready")
        rstd_ready = sem("rstd_ready")
        scaled = sem("scaled")
        normed = sem("normed")

        def landed(batch, i):
            return 16 * ((NLOAD // NSTAGE) * batch + i // NSTAGE + 1)

        def load_role(eng, batch):
            return eng.value_load(roles_sb[0:1, bass.ds(batch, 1)], min_val=0, max_val=R - 1)

        def is_first(batch):
            return isinstance(batch, int) and batch == 0

        def is_last(batch):
            return isinstance(batch, int) and batch == B - 1

        block = ctx.enter_context(nc.Block())

        @block.sync
        def _(sp):
            def load_x_part(batch, i):
                sp.dma_start(x_stage[:, i % NSTAGE, :],
                             xT[batch].rearrange("(p n c) s -> p n (c s)", n=NLOAD, c=CPL)[:, i, :]
                             ).then_inc(x_landed[i % NSTAGE], 16)

            def load_wd_part(role, i):
                sp.dma_start(wd_stage[:, i % NSTAGE, :],
                             W_down[role].rearrange("(p n c) k -> p n (c k)", n=NLOAD, c=CPL)[:, i, :]
                             ).then_inc(wd_landed[i % NSTAGE], 16)

            def load_wu_part(role, i):
                sp.dma_start(wu_stage[:, i % NSTAGE, :],
                             W_up[role, i * P:(i + 1) * P, :]).then_inc(wu_landed[i % NSTAGE], 16)

            def load_rows(batch, t):
                sp.dma_start(rows[:, t, :], x[batch, t * P:(t + 1) * P, :]).then_inc(rows_landed[t], 16)

            def steps(b):
                first, last = is_first(b), is_last(b)
                role = load_role(sp, b)
                for i in range(NSTAGE, NLOAD):
                    sp.wait_ge(wu_split, KC * b + i - NSTAGE + 1)
                    load_wu_part(role, i)
                if not last:
                    next_role = load_role(sp, b + 1)
                    for i in range(NSTAGE):
                        sp.wait_ge(x_split, NLOAD * b + NLOAD - NSTAGE + i + 1)
                        load_x_part(b + 1, i)
                        sp.wait_ge(wd_split, NLOAD * b + NLOAD - NSTAGE + i + 1)
                        load_wd_part(next_role, i)
                for t in range(NT):
                    if not first:
                        sp.wait_ge(stored[t], 16 * b)
                    load_rows(b, t)
                if not last:
                    for i in range(NSTAGE, NLOAD):
                        sp.wait_ge(x_split, NLOAD * (b + 1) + i - NSTAGE + 1)
                        load_x_part(b + 1, i)
                        sp.wait_ge(wd_split, NLOAD * (b + 1) + i - NSTAGE + 1)
                        load_wd_part(next_role, i)
                    for i in range(NSTAGE):
                        sp.wait_ge(wu_split, KC * b + KC - NSTAGE + i + 1)
                        load_wu_part(next_role, i)
                for t in range(NT):
                    sp.wait_ge(normed, NT * b + t + 1)
                    sp.dma_start(out[b, t * P:(t + 1) * P, :], rows[:, t, :]).then_inc(stored[t], 16)

            sp.dma_start(roles_sb[:, :], roles).then_inc(roles_landed, 16)
            load_x_part(0, 0)
            sp.wait_ge(roles_landed, 16)
            first_role = load_role(sp, 0)
            load_wd_part(first_role, 0)
            load_x_part(0, 1)
            load_wd_part(first_role, 1)
            for i in range(NSTAGE, NLOAD):
                sp.wait_ge(x_split, i - NSTAGE + 1)
                load_x_part(0, i)
                sp.wait_ge(wd_split, i - NSTAGE + 1)
                load_wd_part(first_role, i)
            for i in range(NSTAGE):
                load_wu_part(first_role, i)
            sp.dma_start(b_down_all[:, :], b_down_cols).then_inc(b_down_landed, 16)
            for all_roles, param, param_landed in ((b_up_all, b_up, b_up_landed),
                                                   (gamma_all, gamma, gamma_landed),
                                                   (beta_all, beta, beta_landed)):
                row = param.rearrange("(a r) h -> a (r h)", a=1)
                sp.dma_start(all_roles[:, :], row.to_broadcast((P, R * H))).then_inc(param_landed, 16)
            steps(0)
            with sp.Fori(1, B - 1) as b:
                steps(b)
            steps(B - 1)
            for t in range(NT):
                sp.wait_ge(stored[t], 16 * B)

        @block.tensor
        def _(pe):
            def down(batch, n, c, kc, first, last):
                ks = slice(c * K + kc * P, c * K + (kc + 1) * P)
                ss = slice(c * S, (c + 1) * S)
                bank = down_ps[:, kc, :]
                pe.matmul(bank, wd_hi[:, n, ks], x_hi[:, n, ss], start=first, stop=False)
                pe.matmul(bank, wd_hi[:, n, ks], x_lo[:, n, ss], start=False, stop=False)
                return pe.matmul(bank, wd_lo[:, n, ks], x_hi[:, n, ss], start=False, stop=last)

            def up(t, kc):
                ts = slice(t * P, (t + 1) * P)
                half = [slice(i * BANK, (i + 1) * BANK) for i in range(HALVES)]
                for i in range(HALVES):
                    pe.matmul(up_ps[:, t % 2, half[i]], h_hi[:, kc, ts], wu_hi[:, kc, half[i]],
                              start=(kc == 0), stop=False)
                for i in range(HALVES):
                    pe.matmul(up_ps[:, t % 2, half[i]], h_hi[:, kc, ts], wu_lo[:, kc, half[i]],
                              start=False, stop=False)
                for i in range(HALVES):
                    mm = pe.matmul(up_ps[:, t % 2, half[i]], h_lo[:, kc, ts], wu_hi[:, kc, half[i]],
                                   start=False, stop=(kc == KC - 1))
                return mm

            def steps(b):
                first = is_first(b)
                if not first:
                    pe.wait_ge(h_split, KC * b)
                for n in range(NLOAD // 2):
                    pe.wait_ge(x_split, NLOAD * b + n + 1)
                    pe.wait_ge(wd_split, NLOAD * b + n + 1)
                    for kc in range(KC):
                        for c in range(CPL):
                            mm = down(b, n, c, kc, first=(n == 0 and c == 0), last=False)
                    mm.then_inc(d_part_used, 1)
                pe.wait_ge(x_split, NLOAD * (b + 1))
                pe.wait_ge(wd_split, NLOAD * (b + 1))
                for kc in range(KC):
                    for n in range(NLOAD // 2, NLOAD):
                        for c in range(CPL):
                            mm = down(b, n, c, kc, first=False, last=(n == NLOAD - 1 and c == CPL - 1))
                    mm.then_inc(down_ready, 1)
                for t in range(NT):
                    if t < 2:
                        if not first:
                            pe.wait_ge(summed, NT * b)
                    else:
                        pe.wait_ge(summed, NT * b + t - 1)
                    for kc in range(KC):
                        if t == 0:
                            pe.wait_ge(wu_split, KC * b + kc + 1)
                            pe.wait_ge(h_split, KC * b + kc + 1)
                        mm = up(t, kc)
                    mm.then_inc(up_ready, 1)

            steps(0)
            with pe.Fori(1, B - 1) as b:
                steps(b)
            steps(B - 1)

        @block.scalar
        def _(act):
            def round_x_part(batch, i):
                act.wait_ge(x_landed[i % NSTAGE], landed(batch, i))
                act.copy(x_hi[:, i, :], x_stage[:, i % NSTAGE, :]).then_inc(x_hi_ready, 1)

            def round_wd_part(batch, i):
                act.wait_ge(wd_landed[i % NSTAGE], landed(batch, i))
                act.copy(wd_hi[:, i, :], wd_stage[:, i % NSTAGE, :]).then_inc(wd_hi_ready, 1)

            def round_next_part(b, i):
                if i < NLOAD // 2:
                    act.wait_ge(d_part_used, (NLOAD // 2) * b + i + 1)
                else:
                    act.wait_ge(down_ready, KC * (b + 1))
                round_x_part(b + 1, i)
                round_wd_part(b + 1, i)

            def steps(b):
                first, last = is_first(b), is_last(b)
                role = load_role(act, b)
                if not first:
                    act.wait_ge(up_ready, NT * b)
                for i in range(KC):
                    act.wait_ge(wu_landed[i % NSTAGE], landed(b, i))
                    act.copy(wu_hi[:, i, :], wu_stage[:, i % NSTAGE, :]).then_inc(wu_hi_ready, 1)
                for kc in range(KC):
                    if not last and kc < NLOAD // 2:
                        round_next_part(b, kc)
                    act.wait_ge(down_ready, KC * b + kc + 1)
                    if not first:
                        act.wait_ge(h_split, KC * b)
                    bias = b_down_all[:, bass.ds(role * KC + kc, 1)]
                    act.activation(h_full[:, kc, :], down_ps[:, kc, :], ACT.Gelu,
                                   bias=bias).then_inc(h_full_ready, 1)
                    act.wait_ge(h_full_ready, KC * b + kc + 1)
                    act.copy(h_hi[:, kc, :], h_full[:, kc, :]).then_inc(h_hi_ready, 1)
                if not last:
                    for i in range(NLOAD // 2, NLOAD):
                        round_next_part(b, i)

            act.wait_ge(roles_landed, 16)
            for i in range(NLOAD):
                round_x_part(0, i)
                round_wd_part(0, i)
            act.wait_ge(b_down_landed, 16)
            steps(0)
            with act.Fori(1, B - 1) as b:
                steps(b)
            steps(B - 1)

        @block.gpsimd
        def _(pool):
            def steps(b):
                role = load_role(pool, b)
                for t in range(NT):
                    pool.wait_ge(b_up_landed, 16)
                    pool.wait_ge(rows_landed[t], 16 * (b + 1))
                    pool.tensor_tensor(rows[:, t, :], rows[:, t, :], b_up_all[:, bass.ds(role * H, H)],
                                       ALU.add).then_inc(biased, 1)
                for t in range(NT):
                    pool.wait_ge(mean_ready, NT * b + t + 1)
                    pool.tensor_tensor(var_eps[:, t:t + 1], mean_var[:, t, 1:2], eps[:, :],
                                       ALU.add).then_inc(var_eps_ready, 1)
                    pool.wait_ge(var_eps_ready, NT * b + t + 1)
                    pool.tensor_tensor(rstd[:, t:t + 1], var_eps[:, t:t + 1], minus_half[:, :],
                                       ALU.pow).then_inc(rstd_ready, 1)

            pool.memset(eps[:, :], LN_EPS).then_inc(constants_ready, 1)
            pool.memset(minus_half[:, :], -0.5).then_inc(constants_ready, 1)
            pool.wait_ge(constants_ready, 2)
            pool.wait_ge(roles_landed, 16)
            steps(0)
            with pool.Fori(1, B - 1) as b:
                steps(b)
            steps(B - 1)

        @block.vector
        def _(dve):
            def split_x_part(batch, i):
                dve.wait_ge(x_hi_ready, NLOAD * batch + i + 1)
                dve.tensor_tensor(x_lo[:, i, :], x_stage[:, i % NSTAGE, :], x_hi[:, i, :].bitcast(F32),
                                  ALU.subtract).then_inc(x_split, 1)

            def split_wd_part(batch, i):
                dve.wait_ge(wd_hi_ready, NLOAD * batch + i + 1)
                dve.tensor_tensor(wd_lo[:, i, :], wd_stage[:, i % NSTAGE, :], wd_hi[:, i, :].bitcast(F32),
                                  ALU.subtract).then_inc(wd_split, 1)

            def split_next_part(b, i):
                split_x_part(b + 1, i)
                split_wd_part(b + 1, i)

            def sum_tile(b, t):
                dve.wait_ge(biased, NT * b + t + 1)
                dve.wait_ge(up_ready, NT * b + t + 1)
                dve.tensor_tensor(rows[:, t, :], up_ps[:, t % 2, :], rows[:, t, :],
                                  ALU.add).then_inc(summed, 1)

            def norm_tile(b, t, role):
                tiles = NT * b + t + 1
                dve.wait_ge(summed, tiles)
                for i in range(HALVES):
                    stats = dve.bn_stats(bn_parts[:, t, i, :], rows[:, t, i * BANK:(i + 1) * BANK])
                stats.then_inc(bn_ready, 1)
                dve.wait_ge(gamma_landed, 16)
                dve.wait_ge(beta_landed, 16)
                dve.wait_ge(bn_ready, tiles)
                dve.bn_aggr(mean_var[:, t, :], bn_parts[:, t, :, :]).then_inc(mean_ready, 1)
                dve.wait_ge(mean_ready, tiles)
                dve.scalar_tensor_tensor(out=rows[:, t, :], in0=rows[:, t, :], scalar=mean_var[:, t, 0:1],
                                         in1=gamma_all[:, bass.ds(role * H, H)],
                                         op0=ALU.subtract, op1=ALU.mult).then_inc(scaled, 1)
                dve.wait_ge(rstd_ready, tiles)
                dve.wait_ge(scaled, tiles)
                dve.scalar_tensor_tensor(out=rows[:, t, :], in0=rows[:, t, :], scalar=rstd[:, t:t + 1],
                                         in1=beta_all[:, bass.ds(role * H, H)],
                                         op0=ALU.mult, op1=ALU.add).then_inc(normed, 1)

            def steps(b):
                first, last = is_first(b), is_last(b)
                role = load_role(dve, b)
                for i in range(KC):
                    dve.wait_ge(wu_hi_ready, KC * b + i + 1)
                    dve.tensor_tensor(wu_lo[:, i, :], wu_stage[:, i % NSTAGE, :], wu_hi[:, i, :].bitcast(F32),
                                      ALU.subtract).then_inc(wu_split, 1)
                for kc in range(KC):
                    if not last and kc < NLOAD // 2:
                        split_next_part(b, kc)
                    dve.wait_ge(h_hi_ready, KC * b + kc + 1)
                    dve.tensor_tensor(h_lo[:, kc, :], h_full[:, kc, :], h_hi[:, kc, :].bitcast(F32),
                                      ALU.subtract).then_inc(h_split, 1)
                for t in range(NT):
                    if not last and t < NLOAD // 2:
                        split_next_part(b, NLOAD // 2 + t)
                    sum_tile(b, t)
                    norm_tile(b, t, role)

            dve.wait_ge(roles_landed, 16)
            for i in range(NLOAD):
                split_x_part(0, i)
                split_wd_part(0, i)
            steps(0)
            with dve.Fori(1, B - 1) as b:
                steps(b)
            steps(B - 1)


def kernel(**inputs):
    import numpy as np
    import concourse.bacc as bacc
    from concourse.bass_utils import run_bass_kernel_spmd

    x = np.ascontiguousarray(inputs["x"])
    roles = np.ascontiguousarray(inputs["itok_B_1_2"])
    b_down = np.ascontiguousarray(inputs["L0_cond_b_down"])
    R, K = b_down.shape
    arrays = {
        "x": x,
        "xT": np.ascontiguousarray(x.transpose(0, 2, 1)),
        "roles": roles.reshape(1, -1),
        "W_down": np.ascontiguousarray(inputs["L0_cond_W_down"]),
        "b_down_cols": np.ascontiguousarray(b_down.reshape(R, K // P, P).transpose(2, 0, 1).reshape(P, -1)),
        "W_up": np.ascontiguousarray(inputs["L0_cond_W_up"]),
        "b_up": np.ascontiguousarray(inputs["L0_cond_b_up"]),
        "gamma": np.ascontiguousarray(inputs["L0_cond_gamma"]),
        "beta": np.ascontiguousarray(inputs["L0_cond_beta"]),
    }
    nc = bacc.Bacc("TRN2", target_bir_lowering=False, num_devices=1)
    args = [nc.dram_tensor(name, a.shape, mybir.dt.from_np(a.dtype), kind="ExternalInput").ap()
            for name, a in arrays.items()]
    out = nc.dram_tensor("out", x.shape, mybir.dt.from_np(x.dtype), kind="ExternalOutput").ap()
    bass_role_adapter_layernorm(nc, *args, out)
    result = run_bass_kernel_spmd(nc, [arrays], core_ids=[0])
    return result.results[0]["out"]
```

```python
from contextlib import ExitStack

import concourse.bass as bass
from concourse import mybir

P = 128
LN_EPS = 1e-05

ALU = mybir.AluOpType
ACT = mybir.ActivationFunctionType
F32 = mybir.dt.float32
BF16 = mybir.dt.bfloat16
F32R = mybir.dt.float32r
I32 = mybir.dt.int32


def bass_role_adapter_layernorm(
    nc: bass.Bass,
    x: bass.AP,
    xT: bass.AP,
    roles: bass.AP,
    W_down: bass.AP,
    b_down_cols: bass.AP,
    W_up: bass.AP,
    b_up: bass.AP,
    gamma: bass.AP,
    beta: bass.AP,
    out: bass.AP,
):
    B, S, H = x.shape
    R, _, K = W_down.shape
    HC = H // P
    KC = K // P
    NT = S // P
    NLOAD = 4
    CPL = HC // NLOAD
    BANK = 512
    HALVES = H // BANK
    NSTAGE = 2
    assert KC == NLOAD and S == BANK and K == BANK and HALVES == 2 and NT == 4

    with ExitStack() as ctx:
        def sb(name, shape, dt):
            return ctx.enter_context(nc.sbuf_tensor(name, shape, dt))

        def sem(name):
            return ctx.enter_context(nc.semaphore(name))

        x_stage = sb("x_stage", [P, NSTAGE, CPL * S], F32)
        wd_stage = sb("wd_stage", [P, NSTAGE, CPL * K], F32)
        wu_stage = sb("wu_stage", [P, KC, H], F32)
        x_hi = sb("x_hi", [P, NLOAD, CPL * S], F32R)
        x_lo = sb("x_lo", [P, NLOAD, CPL * S], F32R)
        wd_hi = sb("wd_hi", [P, NLOAD, CPL * K], F32R)
        wd_lo = sb("wd_lo", [P, NLOAD, CPL * K], F32R)
        wu_hi = sb("wu_hi", [P, KC, H], F32R)
        wu_lo = sb("wu_lo", [P, KC, H], F32R)
        h_full = sb("h_full", [P, KC, S], F32)
        h_hi = sb("h_hi", [P, KC, S], F32R)
        h_lo = sb("h_lo", [P, KC, S], F32R)
        rows = sb("rows", [P, NT, H], F32)
        b_up_all = sb("b_up_all", [P, R * H], F32)
        gamma_all = sb("gamma_all", [P, R * H], F32)
        beta_all = sb("beta_all", [P, R * H], F32)
        b_down_all = sb("b_down_all", [P, R * KC], F32)
        roles_sb = sb("roles_sb", [1, B], I32)
        row_sum = sb("row_sum", [P, NT], F32)
        neg_mean = sb("neg_mean", [P, NT], F32)
        neg_mean_scaled = sb("neg_mean_scaled", [P, NT], F32)
        squares = sb("squares", [P, H], BF16)
        var = sb("var", [P, NT], F32)
        var_eps = sb("var_eps", [P, NT], F32)
        rstd = sb("rstd", [P, NT], F32)
        eps = sb("eps", [P, 1], F32)
        unused = sb("unused", [P, 1], F32)
        minus_half = sb("minus_half", [P, 1], F32)

        down_ps = ctx.enter_context(nc.psum_tensor("down_ps", [P, KC, BANK], F32))
        up_ps = ctx.enter_context(nc.psum_tensor("up_ps", [P, 2, H], F32))

        roles_landed = sem("roles_landed")
        b_down_landed = sem("b_down_landed")
        params_landed = sem("params_landed")
        x_landed = [sem(f"x_landed{i}") for i in range(NSTAGE)]
        wd_landed = [sem(f"wd_landed{i}") for i in range(NSTAGE)]
        wu_landed = [sem(f"wu_landed{i}") for i in range(KC)]
        rows_landed = [sem(f"rows_landed{t}") for t in range(NT)]
        stored = [sem(f"stored{t}") for t in range(NT)]
        x_hi_ready = sem("x_hi_ready")
        wd_hi_ready = sem("wd_hi_ready")
        wu_hi_ready = sem("wu_hi_ready")
        h_full_ready = sem("h_full_ready")
        h_hi_ready = sem("h_hi_ready")
        x_split = sem("x_split")
        wd_split = sem("wd_split")
        wu_split = sem("wu_split")
        h_split = sem("h_split")
        d_part_used = sem("d_part_used")
        down_ready = sem("down_ready")
        up_ready = sem("up_ready")
        biased = sem("biased")
        summed = sem("summed")
        scaled_mean_ready = sem("scaled_mean_ready")
        mean_ready = sem("mean_ready")
        var_ready = sem("var_ready")
        params_spread = sem("params_spread")
        constants_ready = sem("constants_ready")
        var_eps_ready = sem("var_eps_ready")
        rstd_ready = sem("rstd_ready")
        scaled = sem("scaled")
        normed = sem("normed")

        def landed(batch, i):
            return 16 * ((NLOAD // NSTAGE) * batch + i // NSTAGE + 1)

        def load_role(eng, batch):
            return eng.value_load(roles_sb[0:1, bass.ds(batch, 1)], min_val=0, max_val=R - 1)

        params = [(rows[32 * i:32 * i + 1, :, :].rearrange("p t h -> p (t h)")[:, 0:R * H], all_roles, param)
                  for i, (all_roles, param) in enumerate(((b_up_all, b_up), (gamma_all, gamma), (beta_all, beta)))]

        def is_first(batch):
            return isinstance(batch, int) and batch == 0

        def is_last(batch):
            return isinstance(batch, int) and batch == B - 1

        block = ctx.enter_context(nc.Block())

        @block.sync
        def _(sp):
            def load_x_part(batch, i):
                sp.dma_start(x_stage[:, i % NSTAGE, :],
                             xT[batch].rearrange("(p n c) s -> p n (c s)", n=NLOAD, c=CPL)[:, i, :]
                             ).then_inc(x_landed[i % NSTAGE], 16)

            def load_wd_part(role, i):
                sp.dma_start(wd_stage[:, i % NSTAGE, :],
                             W_down[role].rearrange("(p n c) k -> p n (c k)", n=NLOAD, c=CPL)[:, i, :]
                             ).then_inc(wd_landed[i % NSTAGE], 16)

            def load_wu_part(role, i):
                sp.dma_start(wu_stage[:, i, :],
                             W_up[role, i * P:(i + 1) * P, :]).then_inc(wu_landed[i], 16)

            def load_rows(batch, t):
                sp.dma_start(rows[:, t, :], x[batch, t * P:(t + 1) * P, :]).then_inc(rows_landed[t], 16)

            def steps(b):
                first, last = is_first(b), is_last(b)
                if not last:
                    next_role = load_role(sp, b + 1)
                    for i in range(NSTAGE):
                        sp.wait_ge(x_split, NLOAD * b + NLOAD - NSTAGE + i + 1)
                        load_x_part(b + 1, i)
                        sp.wait_ge(wd_split, NLOAD * b + NLOAD - NSTAGE + i + 1)
                        load_wd_part(next_role, i)
                if first:
                    sp.wait_ge(params_spread, len(params))
                for t in range(NT):
                    if not first:
                        sp.wait_ge(stored[t], 16 * b)
                    load_rows(b, t)
                if not last:
                    for i in range(NSTAGE, NLOAD):
                        sp.wait_ge(x_split, NLOAD * (b + 1) + i - NSTAGE + 1)
                        load_x_part(b + 1, i)
                        sp.wait_ge(wd_split, NLOAD * (b + 1) + i - NSTAGE + 1)
                        load_wd_part(next_role, i)
                    for i in range(KC):
                        sp.wait_ge(wu_split, KC * b + i + 1)
                        load_wu_part(next_role, i)
                for t in range(NT):
                    sp.wait_ge(normed, NT * b + t + 1)
                    sp.dma_start(out[b, t * P:(t + 1) * P, :], rows[:, t, :]).then_inc(stored[t], 16)

            sp.dma_start(roles_sb[:, :], roles).then_inc(roles_landed, 16)
            load_x_part(0, 0)
            sp.wait_ge(roles_landed, 16)
            first_role = load_role(sp, 0)
            load_wd_part(first_role, 0)
            load_x_part(0, 1)
            load_wd_part(first_role, 1)
            sp.dma_start(b_down_all[:, :], b_down_cols).then_inc(b_down_landed, 16)
            for param_row, _, param in params:
                sp.dma_start(param_row, param.rearrange("(a r) h -> a (r h)", a=1)).then_inc(params_landed, 16)
            for i in range(NSTAGE, NLOAD):
                sp.wait_ge(x_split, i - NSTAGE + 1)
                load_x_part(0, i)
                sp.wait_ge(wd_split, i - NSTAGE + 1)
                load_wd_part(first_role, i)
            for i in range(KC):
                load_wu_part(first_role, i)
            steps(0)
            with sp.Fori(1, B - 1) as b:
                steps(b)
            steps(B - 1)
            for t in range(NT):
                sp.wait_ge(stored[t], 16 * B)

        @block.tensor
        def _(pe):
            PASSES = ((wd_hi, x_hi), (wd_hi, x_lo), (wd_lo, x_hi))

            def down(n, c, kc, down_pass, start=False, stop=False):
                wd_part, x_part = PASSES[down_pass]
                return pe.matmul(down_ps[:, kc, :], wd_part[:, n, c * K + kc * P:c * K + (kc + 1) * P],
                                 x_part[:, n, c * S:(c + 1) * S], start=start, stop=stop)

            def up(t, kc):
                ts = slice(t * P, (t + 1) * P)
                half = [slice(i * BANK, (i + 1) * BANK) for i in range(HALVES)]
                for i in range(HALVES):
                    pe.matmul(up_ps[:, t % 2, half[i]], h_hi[:, kc, ts], wu_hi[:, kc, half[i]],
                              start=(kc == 0), stop=False)
                for i in range(HALVES):
                    pe.matmul(up_ps[:, t % 2, half[i]], h_hi[:, kc, ts], wu_lo[:, kc, half[i]],
                              start=False, stop=False)
                for i in range(HALVES):
                    mm = pe.matmul(up_ps[:, t % 2, half[i]], h_lo[:, kc, ts], wu_hi[:, kc, half[i]],
                                   start=False, stop=(kc == KC - 1))
                return mm

            def steps(b):
                first = is_first(b)
                if not first:
                    pe.wait_ge(h_split, KC * b)
                for n in range(NLOAD // 2):
                    parts = NLOAD * b + n + 1
                    for down_pass, needs in enumerate(((x_hi_ready, wd_hi_ready), (x_split,), (wd_split,))):
                        for part_ready in needs:
                            pe.wait_ge(part_ready, parts)
                        for kc in range(KC):
                            for c in range(CPL):
                                mm = down(n, c, kc, down_pass, start=(n == 0 and down_pass == 0 and c == 0))
                    mm.then_inc(d_part_used, 1)
                pe.wait_ge(x_split, NLOAD * (b + 1))
                pe.wait_ge(wd_split, NLOAD * (b + 1))
                for kc in range(KC):
                    for n in range(NLOAD // 2, NLOAD):
                        for c in range(CPL):
                            for down_pass in range(len(PASSES)):
                                mm = down(n, c, kc, down_pass,
                                          stop=(n == NLOAD - 1 and c == CPL - 1 and down_pass == len(PASSES) - 1))
                    mm.then_inc(down_ready, 1)
                for t in range(NT):
                    if t < 2:
                        if not first:
                            pe.wait_ge(summed, NT * b)
                    else:
                        pe.wait_ge(summed, NT * b + t - 1)
                    for kc in range(KC):
                        if t == 0:
                            pe.wait_ge(wu_split, KC * b + kc + 1)
                            pe.wait_ge(h_split, KC * b + kc + 1)
                        mm = up(t, kc)
                    mm.then_inc(up_ready, 1)

            steps(0)
            with pe.Fori(1, B - 1) as b:
                steps(b)
            steps(B - 1)

        @block.scalar
        def _(act):
            def round_x_part(batch, i):
                act.wait_ge(x_landed[i % NSTAGE], landed(batch, i))
                act.copy(x_hi[:, i, :], x_stage[:, i % NSTAGE, :]).then_inc(x_hi_ready, 1)

            def round_wd_part(batch, i):
                act.wait_ge(wd_landed[i % NSTAGE], landed(batch, i))
                act.copy(wd_hi[:, i, :], wd_stage[:, i % NSTAGE, :]).then_inc(wd_hi_ready, 1)

            def round_next_part(b, i):
                if i < NLOAD // 2:
                    act.wait_ge(d_part_used, (NLOAD // 2) * b + i + 1)
                else:
                    act.wait_ge(down_ready, KC * (b + 1))
                round_x_part(b + 1, i)
                round_wd_part(b + 1, i)

            def variance(b, t):
                tiles = NT * b + t + 1
                act.wait_ge(summed, tiles)
                act.mul(neg_mean_scaled[:, t:t + 1], row_sum[:, t:t + 1], -1.0 / H * H ** -0.5).then_inc(scaled_mean_ready, 1)
                act.mul(neg_mean[:, t:t + 1], row_sum[:, t:t + 1], -1.0 / H).then_inc(mean_ready, 1)
                act.wait_ge(scaled_mean_ready, tiles)
                act.activation(squares[:, :], rows[:, t, :], ACT.Square, bias=neg_mean_scaled[:, t:t + 1],
                               scale=H ** -0.5, accum_out=var[:, t:t + 1]).then_inc(var_ready, 1)

            def steps(b):
                first, last = is_first(b), is_last(b)
                role = load_role(act, b)
                if not first:
                    act.wait_ge(up_ready, NT * b)
                for i in range(KC):
                    act.wait_ge(wu_landed[i], 16 * (b + 1))
                    act.copy(wu_hi[:, i, :], wu_stage[:, i, :]).then_inc(wu_hi_ready, 1)
                for kc in range(KC):
                    if not last and kc < NLOAD // 2:
                        round_next_part(b, kc)
                    act.wait_ge(down_ready, KC * b + kc + 1)
                    if not first:
                        act.wait_ge(h_split, KC * b)
                    bias = b_down_all[:, bass.ds(role * KC + kc, 1)]
                    act.activation(h_full[:, kc, :], down_ps[:, kc, :], ACT.Gelu,
                                   bias=bias).then_inc(h_full_ready, 1)
                    act.wait_ge(h_full_ready, KC * b + kc + 1)
                    act.copy(h_hi[:, kc, :], h_full[:, kc, :]).then_inc(h_hi_ready, 1)
                if not last:
                    for i in range(NLOAD // 2, NLOAD):
                        round_next_part(b, i)
                for t in range(NT):
                    variance(b, t)

            act.wait_ge(constants_ready, 2)
            act.activation(unused[:, :], eps[:, :], ACT.Gelu)
            act.wait_ge(roles_landed, 16)
            for i in range(NLOAD):
                round_x_part(0, i)
                round_wd_part(0, i)
            act.wait_ge(b_down_landed, 16)
            steps(0)
            with act.Fori(1, B - 1) as b:
                steps(b)
            steps(B - 1)

        @block.gpsimd
        def _(pool):
            def steps(b):
                role = load_role(pool, b)
                for t in range(NT):
                    pool.wait_ge(params_spread, len(params))
                    pool.wait_ge(rows_landed[t], 16 * (b + 1))
                    pool.tensor_tensor(rows[:, t, :], rows[:, t, :], b_up_all[:, bass.ds(role * H, H)],
                                       ALU.add).then_inc(biased, 1)
                for t in range(NT):
                    pool.wait_ge(var_ready, NT * b + t + 1)
                    pool.tensor_tensor(var_eps[:, t:t + 1], var[:, t:t + 1], eps[:, :],
                                       ALU.add).then_inc(var_eps_ready, 1)
                    pool.wait_ge(var_eps_ready, NT * b + t + 1)
                    pool.tensor_tensor(rstd[:, t:t + 1], var_eps[:, t:t + 1], minus_half[:, :],
                                       ALU.pow).then_inc(rstd_ready, 1)

            pool.memset(eps[:, :], LN_EPS).then_inc(constants_ready, 1)
            pool.memset(minus_half[:, :], -0.5).then_inc(constants_ready, 1)
            pool.wait_ge(constants_ready, 2)
            pool.wait_ge(params_landed, 16 * len(params))
            for param_row, all_roles, _ in params:
                pool.partition_broadcast(all_roles[:, :], param_row).then_inc(params_spread, 1)
            pool.wait_ge(roles_landed, 16)
            steps(0)
            with pool.Fori(1, B - 1) as b:
                steps(b)
            steps(B - 1)

        @block.vector
        def _(dve):
            def split_x_part(batch, i):
                dve.wait_ge(x_hi_ready, NLOAD * batch + i + 1)
                dve.tensor_tensor(x_lo[:, i, :], x_stage[:, i % NSTAGE, :], x_hi[:, i, :].bitcast(F32),
                                  ALU.subtract).then_inc(x_split, 1)

            def split_wd_part(batch, i):
                dve.wait_ge(wd_hi_ready, NLOAD * batch + i + 1)
                dve.tensor_tensor(wd_lo[:, i, :], wd_stage[:, i % NSTAGE, :], wd_hi[:, i, :].bitcast(F32),
                                  ALU.subtract).then_inc(wd_split, 1)

            def split_next_part(b, i):
                split_x_part(b + 1, i)
                split_wd_part(b + 1, i)

            def sum_tile(b, t):
                dve.wait_ge(biased, NT * b + t + 1)
                dve.wait_ge(up_ready, NT * b + t + 1)
                dve.scalar_tensor_tensor(out=rows[:, t, :], in0=up_ps[:, t % 2, :], scalar=1.0,
                                         in1=rows[:, t, :], op0=ALU.mult, op1=ALU.add,
                                         accum_out=row_sum[:, t:t + 1]).then_inc(summed, 1)

            def norm_tile(b, t, role):
                tiles = NT * b + t + 1
                dve.wait_ge(params_spread, len(params))
                dve.wait_ge(mean_ready, tiles)
                dve.wait_ge(var_ready, tiles)
                dve.scalar_tensor_tensor(out=rows[:, t, :], in0=rows[:, t, :], scalar=neg_mean[:, t:t + 1],
                                         in1=gamma_all[:, bass.ds(role * H, H)],
                                         op0=ALU.add, op1=ALU.mult).then_inc(scaled, 1)
                dve.wait_ge(rstd_ready, tiles)
                dve.wait_ge(scaled, tiles)
                dve.scalar_tensor_tensor(out=rows[:, t, :], in0=rows[:, t, :], scalar=rstd[:, t:t + 1],
                                         in1=beta_all[:, bass.ds(role * H, H)],
                                         op0=ALU.mult, op1=ALU.add).then_inc(normed, 1)

            def steps(b):
                first, last = is_first(b), is_last(b)
                role = load_role(dve, b)
                for i in range(KC):
                    dve.wait_ge(wu_hi_ready, KC * b + i + 1)
                    dve.tensor_tensor(wu_lo[:, i, :], wu_stage[:, i, :], wu_hi[:, i, :].bitcast(F32),
                                      ALU.subtract).then_inc(wu_split, 1)
                for kc in range(KC):
                    if not last and kc < NLOAD // 2:
                        split_next_part(b, kc)
                    dve.wait_ge(h_hi_ready, KC * b + kc + 1)
                    dve.tensor_tensor(h_lo[:, kc, :], h_full[:, kc, :], h_hi[:, kc, :].bitcast(F32),
                                      ALU.subtract).then_inc(h_split, 1)
                if not last:
                    for i in range(NLOAD // 2, NLOAD):
                        split_next_part(b, i)
                for t in range(NT):
                    sum_tile(b, t)
                    if t > 0:
                        norm_tile(b, t - 1, role)
                norm_tile(b, NT - 1, role)

            dve.wait_ge(roles_landed, 16)
            for i in range(NLOAD):
                split_x_part(0, i)
                split_wd_part(0, i)
            steps(0)
            with dve.Fori(1, B - 1) as b:
                steps(b)
            steps(B - 1)


def kernel(**inputs):
    import numpy as np
    import concourse.bacc as bacc
    from concourse.bass_utils import run_bass_kernel_spmd

    x = np.ascontiguousarray(inputs["x"])
    roles = np.ascontiguousarray(inputs["itok_B_1_2"])
    b_down = np.ascontiguousarray(inputs["L0_cond_b_down"])
    R, K = b_down.shape
    arrays = {
        "x": x,
        "xT": np.ascontiguousarray(x.transpose(0, 2, 1)),
        "roles": roles.reshape(1, -1),
        "W_down": np.ascontiguousarray(inputs["L0_cond_W_down"]),
        "b_down_cols": np.ascontiguousarray(b_down.reshape(R, K // P, P).transpose(2, 0, 1).reshape(P, -1)),
        "W_up": np.ascontiguousarray(inputs["L0_cond_W_up"]),
        "b_up": np.ascontiguousarray(inputs["L0_cond_b_up"]),
        "gamma": np.ascontiguousarray(inputs["L0_cond_gamma"]),
        "beta": np.ascontiguousarray(inputs["L0_cond_beta"]),
    }
    nc = bacc.Bacc("TRN2", target_bir_lowering=False, num_devices=1)
    args = [nc.dram_tensor(name, a.shape, mybir.dt.from_np(a.dtype), kind="ExternalInput").ap()
            for name, a in arrays.items()]
    out = nc.dram_tensor("out", x.shape, mybir.dt.from_np(x.dtype), kind="ExternalOutput").ap()
    bass_role_adapter_layernorm(nc, *args, out)
    result = run_bass_kernel_spmd(nc, [arrays], core_ids=[0])
    return result.results[0]["out"]
```

```python
from contextlib import ExitStack

import concourse.bass as bass
from concourse import mybir

P = 128
LN_EPS = 1e-05

ALU = mybir.AluOpType
ACT = mybir.ActivationFunctionType
F32 = mybir.dt.float32
BF16 = mybir.dt.bfloat16
F32R = mybir.dt.float32r
I32 = mybir.dt.int32


def bass_role_adapter_layernorm(
    nc: bass.Bass,
    x: bass.AP,
    xT: bass.AP,
    roles: bass.AP,
    W_down: bass.AP,
    b_down_cols: bass.AP,
    W_up: bass.AP,
    b_up: bass.AP,
    gamma: bass.AP,
    beta: bass.AP,
    out: bass.AP,
):
    B, S, H = x.shape
    R, _, K = W_down.shape
    HC = H // P
    KC = K // P
    NT = S // P
    NLOAD = 4
    CPL = HC // NLOAD
    BANK = 512
    HALVES = H // BANK
    NSTAGE = 2
    WARM_UP = 12
    assert KC == NLOAD and S == BANK and K == BANK and HALVES == 2 and NT == 4

    with ExitStack() as ctx:
        def sb(name, shape, dt):
            return ctx.enter_context(nc.sbuf_tensor(name, shape, dt))

        def sem(name):
            return ctx.enter_context(nc.semaphore(name))

        x_stage = sb("x_stage", [P, NSTAGE, CPL * S], F32)
        wd_stage = sb("wd_stage", [P, NSTAGE, CPL * K], F32)
        wu_stage = sb("wu_stage", [P, KC, H], F32)
        x_hi = sb("x_hi", [P, NLOAD, CPL * S], F32R)
        x_lo = sb("x_lo", [P, NLOAD, CPL * S], F32R)
        wd_hi = sb("wd_hi", [P, NLOAD, CPL * K], F32R)
        wd_lo = sb("wd_lo", [P, NLOAD, CPL * K], F32R)
        wu_hi = sb("wu_hi", [P, KC, H], F32R)
        wu_lo = sb("wu_lo", [P, KC, H], F32R)
        h_full = sb("h_full", [P, KC, S], F32)
        h_hi = sb("h_hi", [P, KC, S], F32R)
        h_lo = sb("h_lo", [P, KC, S], F32R)
        rows = sb("rows", [P, NT, H], F32)
        b_up_all = sb("b_up_all", [P, R * H], F32)
        gamma_all = sb("gamma_all", [P, R * H], F32)
        beta_all = sb("beta_all", [P, R * H], F32)
        b_down_all = sb("b_down_all", [P, R * KC], F32)
        roles_sb = sb("roles_sb", [1, B], I32)
        row_sum = sb("row_sum", [P, NT], F32)
        neg_mean = sb("neg_mean", [P, NT], F32)
        neg_mean_scaled = sb("neg_mean_scaled", [P, NT], F32)
        half_sums = sb("half_sums", [P, HALVES], F32)
        half_means = sb("half_means", [P, 2], F32)
        squares = sb("squares", [P, H], BF16)
        var = sb("var", [P, NT, HALVES], F32)
        var_eps = sb("var_eps", [P, NT, 2], F32)
        rstd = sb("rstd", [P, NT], F32)
        eps = sb("eps", [P, 1], F32)
        unused = sb("unused", [P, 1], F32)
        minus_half = sb("minus_half", [P, 1], F32)

        down_ps = ctx.enter_context(nc.psum_tensor("down_ps", [P, KC, BANK], F32))
        up_ps = ctx.enter_context(nc.psum_tensor("up_ps", [P, 2, H], F32))

        roles_landed = sem("roles_landed")
        b_down_landed = sem("b_down_landed")
        params_landed = sem("params_landed")
        x_landed = [sem(f"x_landed{i}") for i in range(NSTAGE)]
        wd_landed = [sem(f"wd_landed{i}") for i in range(NSTAGE)]
        first_chunk_landed = sem("first_chunk_landed")
        wu_landed = [sem(f"wu_landed{i}") for i in range(KC)]
        rows_landed = [sem(f"rows_landed{t}") for t in range(NT)]
        stored = [sem(f"stored{t}") for t in range(NT)]
        last_stored = sem("last_stored")
        x_hi_ready = sem("x_hi_ready")
        wd_hi_ready = sem("wd_hi_ready")
        first_chunk_hi = sem("first_chunk_hi")
        wu_hi_ready = sem("wu_hi_ready")
        h_full_ready = sem("h_full_ready")
        h_hi_ready = sem("h_hi_ready")
        x_split = sem("x_split")
        wd_split = sem("wd_split")
        wu_split = sem("wu_split")
        h_split = sem("h_split")
        d_part_used = sem("d_part_used")
        down_ready = sem("down_ready")
        up_ready = sem("up_ready")
        last_half_ready = sem("last_half_ready")
        biased = sem("biased")
        summed = sem("summed")
        last_half_summed = sem("last_half_summed")
        half_means_ready = sem("half_means_ready")
        scaled_mean_ready = sem("scaled_mean_ready")
        mean_ready = sem("mean_ready")
        var_ready = sem("var_ready")
        half_var_eps_ready = sem("half_var_eps_ready")
        params_spread = sem("params_spread")
        zeros_ready = sem("zeros_ready")
        constants_ready = sem("constants_ready")
        var_eps_ready = sem("var_eps_ready")
        rstd_ready = sem("rstd_ready")
        scaled = sem("scaled")
        normed = sem("normed")

        def landed(batch, i):
            return 16 * ((NLOAD // NSTAGE) * batch + i // NSTAGE + 1)

        def load_role(eng, batch):
            return eng.value_load(roles_sb[0:1, bass.ds(batch, 1)], min_val=0, max_val=R - 1)

        params = [(rows[32 * i:32 * i + 1, :, :].rearrange("p t h -> p (t h)")[:, 0:R * H], all_roles, param)
                  for i, (all_roles, param) in enumerate(((b_up_all, b_up), (gamma_all, gamma), (beta_all, beta)))]

        centred = h_full[:, :, :].rearrange("p (t i) s -> p t (i s)", t=2)

        def is_first(batch):
            return isinstance(batch, int) and batch == 0

        def is_last(batch):
            return isinstance(batch, int) and batch == B - 1

        block = ctx.enter_context(nc.Block())

        @block.sync
        def _(sp):
            def load_x_part(batch, i):
                sp.dma_start(x_stage[:, i % NSTAGE, :],
                             xT[batch].rearrange("(p n c) s -> p n (c s)", n=NLOAD, c=CPL)[:, i, :]
                             ).then_inc(x_landed[i % NSTAGE], 16)

            def load_wd_part(role, i):
                sp.dma_start(wd_stage[:, i % NSTAGE, :],
                             W_down[role].rearrange("(p n c) k -> p n (c k)", n=NLOAD, c=CPL)[:, i, :]
                             ).then_inc(wd_landed[i % NSTAGE], 16)

            def load_first_wd_part(role):
                src = W_down[role].rearrange("(p c) k -> p (c k)", c=HC)
                sp.dma_start(wd_stage[:, 0, 0:K], src[:, 0:K]).then_inc(first_chunk_landed, 16)
                sp.dma_start(wd_stage[:, 0, K:CPL * K], src[:, K:CPL * K]).then_inc(wd_landed[0], 16)

            def load_wu_part(role, i):
                sp.dma_start(wu_stage[:, i, :],
                             W_up[role, i * P:(i + 1) * P, :]).then_inc(wu_landed[i], 16)

            def load_rows(batch, t):
                sp.dma_start(rows[:, t, :], x[batch, t * P:(t + 1) * P, :]).then_inc(rows_landed[t], 16)

            def steps(b):
                first, last = is_first(b), is_last(b)
                if not last:
                    next_role = load_role(sp, b + 1)
                    for i in range(NSTAGE):
                        sp.wait_ge(x_split, NLOAD * b + NLOAD - NSTAGE + i + 1)
                        load_x_part(b + 1, i)
                        sp.wait_ge(wd_split, NLOAD * b + NLOAD - NSTAGE + i + 1)
                        load_wd_part(next_role, i)
                if first:
                    sp.wait_ge(params_spread, len(params))
                for t in range(NT):
                    if not first:
                        sp.wait_ge(stored[t], 16 * b)
                    load_rows(b, t)
                    if not last and t in (1, 2):
                        i = NLOAD // 2 + t - 1
                        sp.wait_ge(x_split, NLOAD * (b + 1) + i - NSTAGE + 1)
                        load_x_part(b + 1, i)
                        sp.wait_ge(wd_split, NLOAD * (b + 1) + i - NSTAGE + 1)
                        load_wd_part(next_role, i)
                if not last:
                    for i in range(KC):
                        sp.wait_ge(wu_split, KC * b + i + 1)
                        load_wu_part(next_role, i)
                for t in range(NT):
                    if is_last(b) and t == NT - 1:
                        for i in range(HALVES):
                            sp.wait_ge(normed, NT * B + i)
                            half = slice(i * BANK, (i + 1) * BANK)
                            sp.dma_start(out[b, t * P:(t + 1) * P, half], rows[:, t, half]).then_inc(last_stored, 16)
                        continue
                    sp.wait_ge(normed, NT * b + t + 1)
                    sp.dma_start(out[b, t * P:(t + 1) * P, :], rows[:, t, :]).then_inc(stored[t], 16)

            sp.dma_start(roles_sb[:, :], roles).then_inc(roles_landed, 16)
            load_x_part(0, 0)
            sp.wait_ge(roles_landed, 16)
            first_role = load_role(sp, 0)
            load_first_wd_part(first_role)
            load_x_part(0, 1)
            load_wd_part(first_role, 1)
            sp.dma_start(b_down_all[:, :], b_down_cols).then_inc(b_down_landed, 16)
            for param_row, _, param in params:
                sp.dma_start(param_row, param.rearrange("(a r) h -> a (r h)", a=1)).then_inc(params_landed, 16)
            for i in range(NSTAGE, NLOAD):
                sp.wait_ge(x_split, i - NSTAGE + 1)
                load_x_part(0, i)
                sp.wait_ge(wd_split, i - NSTAGE + 1)
                load_wd_part(first_role, i)
            for i in range(KC):
                load_wu_part(first_role, i)
            steps(0)
            with sp.Fori(1, B - 1) as b:
                steps(b)
            steps(B - 1)
            for t in range(NT - 1):
                sp.wait_ge(stored[t], 16 * B)
            sp.wait_ge(stored[NT - 1], 16 * (B - 1))
            sp.wait_ge(last_stored, 16 * HALVES)

        @block.tensor
        def _(pe):
            PASSES = ((wd_hi, x_hi), (wd_hi, x_lo), (wd_lo, x_hi))

            def down(n, c, kc, down_pass, start=False, stop=False):
                wd_part, x_part = PASSES[down_pass]
                return pe.matmul(down_ps[:, kc, :], wd_part[:, n, c * K + kc * P:c * K + (kc + 1) * P],
                                 x_part[:, n, c * S:(c + 1) * S], start=start, stop=stop)

            def up(t, kc, halves=range(HALVES)):
                for h_part, wu_part in ((h_hi, wu_hi), (h_hi, wu_lo), (h_lo, wu_hi)):
                    for i in halves:
                        half = slice(i * BANK, (i + 1) * BANK)
                        mm = pe.matmul(up_ps[:, t % 2, half], h_part[:, kc, t * P:(t + 1) * P], wu_part[:, kc, half],
                                       start=(kc == 0 and h_part is h_hi and wu_part is wu_hi),
                                       stop=(kc == KC - 1 and h_part is h_lo))
                return mm

            def steps(b):
                first = is_first(b)
                if not first:
                    pe.wait_ge(h_split, KC * b)
                for n in range(NLOAD // 2):
                    parts = NLOAD * b + n + 1
                    for down_pass, needs in enumerate(((x_hi_ready, wd_hi_ready), (x_split,), (wd_split,))):
                        first_chunk_apart = first and n == 0 and down_pass == 0
                        for part_ready in needs:
                            if not (first_chunk_apart and part_ready is wd_hi_ready):
                                pe.wait_ge(part_ready, parts)
                        for c in range(CPL):
                            if first_chunk_apart and c == 0:
                                pe.wait_ge(first_chunk_hi, 1)
                            elif first_chunk_apart:
                                pe.wait_ge(wd_hi_ready, parts)
                            for kc in range(KC):
                                mm = down(n, c, kc, down_pass, start=(n == 0 and down_pass == 0 and c == 0))
                    mm.then_inc(d_part_used, 1)
                for kc in range(KC):
                    for n in range(NLOAD // 2, NLOAD):
                        if kc == 0:
                            pe.wait_ge(x_split, NLOAD * b + n + 1)
                            pe.wait_ge(wd_split, NLOAD * b + n + 1)
                        for c in range(CPL):
                            for down_pass in range(len(PASSES)):
                                mm = down(n, c, kc, down_pass,
                                          stop=(n == NLOAD - 1 and c == CPL - 1 and down_pass == len(PASSES) - 1))
                    mm.then_inc(down_ready, 1)
                for t in range(NT):
                    if t < 2:
                        if not first:
                            pe.wait_ge(summed, NT * b)
                    else:
                        pe.wait_ge(summed, NT * b + t - 1)
                    if is_last(b) and t == NT - 1:
                        for i in range(HALVES):
                            for kc in range(KC):
                                mm = up(t, kc, [i])
                            mm.then_inc(last_half_ready, 1)
                        continue
                    for kc in range(KC):
                        if t == 0:
                            pe.wait_ge(wu_split, KC * b + kc + 1)
                            pe.wait_ge(h_split, KC * b + kc + 1)
                        mm = up(t, kc)
                    mm.then_inc(up_ready, 1)

            pe.wait_ge(zeros_ready, 1)
            for _ in range(WARM_UP):
                pe.matmul(up_ps[:, 0, 0:BANK], squares[:, 0:P], squares[:, 0:BANK], start=True, stop=True)
            steps(0)
            with pe.Fori(1, B - 1) as b:
                steps(b)
            steps(B - 1)

        @block.scalar
        def _(act):
            def round_x_part(batch, i):
                act.wait_ge(x_landed[i % NSTAGE], landed(batch, i))
                act.copy(x_hi[:, i, :], x_stage[:, i % NSTAGE, :]).then_inc(x_hi_ready, 1)

            def round_wd_part(batch, i):
                act.wait_ge(wd_landed[i % NSTAGE], landed(batch, i))
                act.copy(wd_hi[:, i, :], wd_stage[:, i % NSTAGE, :]).then_inc(wd_hi_ready, 1)

            def round_next_part(b, i):
                if i < NLOAD // 2:
                    act.wait_ge(d_part_used, (NLOAD // 2) * b + i + 1)
                else:
                    act.wait_ge(down_ready, KC * (b + 1))
                round_x_part(b + 1, i)
                round_wd_part(b + 1, i)

            def square_halves(t):
                for i in range(HALVES):
                    half = slice(i * BANK, (i + 1) * BANK)
                    act.activation(squares[:, half], rows[:, t, half], ACT.Square, bias=neg_mean_scaled[:, t:t + 1],
                                   scale=H ** -0.5, accum_out=var[:, t, i:i + 1]).then_inc(var_ready, 1)

            def variance(b, t):
                tiles = NT * b + t + 1
                act.wait_ge(summed, tiles)
                act.mul(neg_mean_scaled[:, t:t + 1], row_sum[:, t:t + 1], -1.0 / H * H ** -0.5).then_inc(scaled_mean_ready, 1)
                act.mul(neg_mean[:, t:t + 1], row_sum[:, t:t + 1], -1.0 / H).then_inc(mean_ready, 1)
                act.wait_ge(scaled_mean_ready, tiles)
                square_halves(t)

            def last_variance():
                t = NT - 1
                act.wait_ge(last_half_summed, 1)
                act.mul(half_means[:, 0:1], half_sums[:, 0:1], -1.0 / H * H ** -0.5).then_inc(half_means_ready, 1)
                act.mul(half_means[:, 1:2], half_sums[:, 0:1], -1.0 / H).then_inc(half_means_ready, 1)
                act.wait_ge(half_means_ready, 2)
                act.wait_ge(last_half_summed, 2)
                act.activation(neg_mean_scaled[:, t:t + 1], half_sums[:, 1:2], ACT.Identity, bias=half_means[:, 0:1],
                               scale=-1.0 / H * H ** -0.5).then_inc(scaled_mean_ready, 1)
                act.activation(neg_mean[:, t:t + 1], half_sums[:, 1:2], ACT.Identity, bias=half_means[:, 1:2],
                               scale=-1.0 / H).then_inc(mean_ready, 1)
                act.wait_ge(scaled_mean_ready, NT * B)
                square_halves(t)

            def steps(b):
                first, last = is_first(b), is_last(b)
                role = load_role(act, b)
                if not first:
                    act.wait_ge(up_ready, NT * b)
                for i in range(KC):
                    act.wait_ge(wu_landed[i], 16 * (b + 1))
                    act.copy(wu_hi[:, i, :], wu_stage[:, i, :]).then_inc(wu_hi_ready, 1)
                for kc in range(KC):
                    act.wait_ge(down_ready, KC * b + kc + 1)
                    if not first:
                        act.wait_ge(normed, NT * b)
                    bias = b_down_all[:, bass.ds(role * KC + kc, 1)]
                    act.activation(h_full[:, kc, :], down_ps[:, kc, :], ACT.Gelu,
                                   bias=bias).then_inc(h_full_ready, 1)
                    act.wait_ge(h_full_ready, KC * b + kc + 1)
                    act.copy(h_hi[:, kc, :], h_full[:, kc, :]).then_inc(h_hi_ready, 1)
                    if not last and kc < NLOAD // 2:
                        round_next_part(b, kc)
                if not last:
                    for i in range(NLOAD // 2, NLOAD):
                        round_next_part(b, i)
                for t in range(NT):
                    if last and t == NT - 1:
                        last_variance()
                    else:
                        variance(b, t)

            act.wait_ge(constants_ready, 2)
            act.activation(unused[:, :], eps[:, :], ACT.Gelu)
            act.wait_ge(roles_landed, 16)
            round_x_part(0, 0)
            act.wait_ge(first_chunk_landed, 16)
            act.copy(wd_hi[:, 0, 0:K], wd_stage[:, 0, 0:K]).then_inc(first_chunk_hi, 1)
            act.wait_ge(wd_landed[0], landed(0, 0))
            act.copy(wd_hi[:, 0, K:CPL * K], wd_stage[:, 0, K:CPL * K]).then_inc(wd_hi_ready, 1)
            for i in range(1, NLOAD):
                round_x_part(0, i)
                round_wd_part(0, i)
            act.wait_ge(b_down_landed, 16)
            steps(0)
            with act.Fori(1, B - 1) as b:
                steps(b)
            steps(B - 1)

        @block.gpsimd
        def _(pool):
            def steps(b):
                role = load_role(pool, b)
                for t in range(NT):
                    pool.wait_ge(params_spread, len(params))
                    pool.wait_ge(rows_landed[t], 16 * (b + 1))
                    pool.tensor_tensor(rows[:, t, :], rows[:, t, :], b_up_all[:, bass.ds(role * H, H)],
                                       ALU.add).then_inc(biased, 1)
                for t in range(NT):
                    pool.wait_ge(var_ready, HALVES * (NT * b + t) + 1)
                    pool.tensor_tensor(var_eps[:, t, 0:1], var[:, t, 0:1], eps[:, :],
                                       ALU.add).then_inc(half_var_eps_ready, 1)
                    pool.wait_ge(half_var_eps_ready, NT * b + t + 1)
                    pool.wait_ge(var_ready, HALVES * (NT * b + t + 1))
                    pool.tensor_tensor(var_eps[:, t, 1:2], var[:, t, 1:2], var_eps[:, t, 0:1],
                                       ALU.add).then_inc(var_eps_ready, 1)
                    pool.wait_ge(var_eps_ready, NT * b + t + 1)
                    pool.tensor_tensor(rstd[:, t:t + 1], var_eps[:, t, 1:2], minus_half[:, :],
                                       ALU.pow).then_inc(rstd_ready, 1)

            pool.memset(eps[:, :], LN_EPS).then_inc(constants_ready, 1)
            pool.memset(minus_half[:, :], -0.5).then_inc(constants_ready, 1)
            pool.wait_ge(constants_ready, 2)
            pool.wait_ge(params_landed, 16 * len(params))
            for param_row, all_roles, _ in params:
                pool.partition_broadcast(all_roles[:, :], param_row).then_inc(params_spread, 1)
            pool.wait_ge(roles_landed, 16)
            steps(0)
            with pool.Fori(1, B - 1) as b:
                steps(b)
            steps(B - 1)

        @block.vector
        def _(dve):
            def split_x_part(batch, i):
                dve.wait_ge(x_hi_ready, NLOAD * batch + i + 1)
                dve.tensor_tensor(x_lo[:, i, :], x_stage[:, i % NSTAGE, :], x_hi[:, i, :].bitcast(F32),
                                  ALU.subtract).then_inc(x_split, 1)

            def split_wd_part(batch, i):
                dve.wait_ge(wd_hi_ready, NLOAD * batch + i + 1)
                dve.tensor_tensor(wd_lo[:, i, :], wd_stage[:, i % NSTAGE, :], wd_hi[:, i, :].bitcast(F32),
                                  ALU.subtract).then_inc(wd_split, 1)

            def split_next_part(b, i):
                split_x_part(b + 1, i)
                split_wd_part(b + 1, i)

            def sum_tile(b, t):
                dve.wait_ge(biased, NT * b + t + 1)
                dve.wait_ge(up_ready, NT * b + t + 1)
                dve.scalar_tensor_tensor(out=rows[:, t, :], in0=up_ps[:, t % 2, :], scalar=1.0,
                                         in1=rows[:, t, :], op0=ALU.mult, op1=ALU.add,
                                         accum_out=row_sum[:, t:t + 1]).then_inc(summed, 1)

            def sum_last_half(i):
                t, half = NT - 1, slice(i * BANK, (i + 1) * BANK)
                dve.wait_ge(biased, NT * B)
                dve.wait_ge(last_half_ready, i + 1)
                dve.scalar_tensor_tensor(out=rows[:, t, half], in0=up_ps[:, t % 2, half], scalar=1.0,
                                         in1=rows[:, t, half], op0=ALU.mult, op1=ALU.add,
                                         accum_out=half_sums[:, i:i + 1]).then_inc(last_half_summed, 1)

            def centre_tile(b, t, role, halves=(slice(0, H),)):
                dve.wait_ge(params_spread, len(params))
                dve.wait_ge(mean_ready, NT * b + t + 1)
                for half in halves:
                    dve.scalar_tensor_tensor(out=centred[:, t % 2, half], in0=rows[:, t, half],
                                             scalar=neg_mean[:, t:t + 1],
                                             in1=gamma_all[:, bass.ds(role * H + half.start, half.stop - half.start)],
                                             op0=ALU.add, op1=ALU.mult).then_inc(scaled, 1)

            def finish_tile(b, t, role, halves=(slice(0, H),)):
                dve.wait_ge(var_ready, HALVES * (NT * b + t + 1))
                dve.wait_ge(rstd_ready, NT * b + t + 1)
                for i, half in enumerate(halves):
                    dve.wait_ge(scaled, NT * b + t + 1 + i)
                    dve.scalar_tensor_tensor(out=rows[:, t, half], in0=centred[:, t % 2, half],
                                             scalar=rstd[:, t:t + 1],
                                             in1=beta_all[:, bass.ds(role * H + half.start, half.stop - half.start)],
                                             op0=ALU.mult, op1=ALU.add).then_inc(normed, 1)

            def last_tiles(role):
                b, halves = B - 1, [slice(i * BANK, (i + 1) * BANK) for i in range(HALVES)]
                for t in range(NT - 2):
                    sum_tile(b, t)
                    centre_tile(b, t, role)
                    finish_tile(b, t, role)
                sum_tile(b, NT - 2)
                centre_tile(b, NT - 2, role)
                sum_last_half(0)
                finish_tile(b, NT - 2, role)
                sum_last_half(1)
                centre_tile(b, NT - 1, role, halves)
                finish_tile(b, NT - 1, role, halves)

            def steps(b):
                last = is_last(b)
                role = load_role(dve, b)
                for i in range(KC):
                    dve.wait_ge(wu_hi_ready, KC * b + i + 1)
                    dve.tensor_tensor(wu_lo[:, i, :], wu_stage[:, i, :], wu_hi[:, i, :].bitcast(F32),
                                      ALU.subtract).then_inc(wu_split, 1)
                for kc in range(KC):
                    dve.wait_ge(h_hi_ready, KC * b + kc + 1)
                    dve.tensor_tensor(h_lo[:, kc, :], h_full[:, kc, :], h_hi[:, kc, :].bitcast(F32),
                                      ALU.subtract).then_inc(h_split, 1)
                    if not last and kc < NLOAD // 2:
                        split_next_part(b, kc)
                if last:
                    last_tiles(role)
                    return
                for t in range(NT):
                    if t < NLOAD // 2:
                        split_next_part(b, NLOAD // 2 + t)
                    sum_tile(b, t)
                    if t > 0:
                        centre_tile(b, t - 1, role)
                        finish_tile(b, t - 1, role)
                centre_tile(b, NT - 1, role)
                finish_tile(b, NT - 1, role)

            dve.memset(squares[:, 0:BANK], 0.0).then_inc(zeros_ready, 1)
            dve.wait_ge(roles_landed, 16)
            for i in range(NLOAD):
                split_x_part(0, i)
                if i == 0:
                    dve.wait_ge(first_chunk_hi, 1)
                split_wd_part(0, i)
            steps(0)
            with dve.Fori(1, B - 1) as b:
                steps(b)
            steps(B - 1)


def kernel(**inputs):
    import numpy as np
    import concourse.bacc as bacc
    from concourse.bass_utils import run_bass_kernel_spmd

    x = np.ascontiguousarray(inputs["x"])
    roles = np.ascontiguousarray(inputs["itok_B_1_2"])
    b_down = np.ascontiguousarray(inputs["L0_cond_b_down"])
    R, K = b_down.shape
    arrays = {
        "x": x,
        "xT": np.ascontiguousarray(x.transpose(0, 2, 1)),
        "roles": roles.reshape(1, -1),
        "W_down": np.ascontiguousarray(inputs["L0_cond_W_down"]),
        "b_down_cols": np.ascontiguousarray(b_down.reshape(R, K // P, P).transpose(2, 0, 1).reshape(P, -1)),
        "W_up": np.ascontiguousarray(inputs["L0_cond_W_up"]),
        "b_up": np.ascontiguousarray(inputs["L0_cond_b_up"]),
        "gamma": np.ascontiguousarray(inputs["L0_cond_gamma"]),
        "beta": np.ascontiguousarray(inputs["L0_cond_beta"]),
    }
    nc = bacc.Bacc("TRN2", target_bir_lowering=False, num_devices=1)
    args = [nc.dram_tensor(name, a.shape, mybir.dt.from_np(a.dtype), kind="ExternalInput").ap()
            for name, a in arrays.items()]
    out = nc.dram_tensor("out", x.shape, mybir.dt.from_np(x.dtype), kind="ExternalOutput").ap()
    bass_role_adapter_layernorm(nc, *args, out)
    result = run_bass_kernel_spmd(nc, [arrays], core_ids=[0])
    return result.results[0]["out"]
```
